# Optimizing a Trainium2 kernel written in Bass

```python
import numpy as np
import jax
import jax.numpy as jnp

def _softmax(x, axis=-1):
    return jax.nn.softmax(x, axis=axis)

def _gelu(x):
    return jax.nn.gelu(x, approximate=True)

def _silu(x):
    return jax.nn.silu(x)

def _sigmoid(x):
    return jax.nn.sigmoid(x)

def _layernorm(x, axis=-1, eps=1e-05):
    m = jnp.mean(x, axis=axis, keepdims=True)
    v = jnp.var(x, axis=axis, keepdims=True)
    return (x - m) / jnp.sqrt(v + eps)

def _scatter_add(tgt, idx, src, axis=0):
    return tgt.at[idx].add(src)

def _segment_sum(src, seg, n):
    return jax.ops.segment_sum(src, seg, n)
kernel_name = 'mk_gnn_resnorm_d2_gnn_r8_901902'

def setup_inputs(seed: int=0):
    np.random.seed(seed)
    _w = jnp.asarray

    def _rec_inputs():
        import jax
        import jax.numpy as jnp
        _gk = jax.random.key(seed)
        x = -0.0005121 + 1.001 * jax.random.normal(jax.random.fold_in(_gk, 1), (6250, 64), jnp.float32)
        src = jax.random.randint(jax.random.fold_in(_gk, 2), (200000,), 0, 6250, jnp.int32)
        dst = jnp.minimum((6250 * jax.random.uniform(jax.random.fold_in(_gk, 3), (200000,)) ** 2.0).astype(jnp.int32), 49999)
        _o = jnp.argsort(dst, stable=True)
        src = src[_o]
        dst = dst[_o]
        return (x, src, dst)
    x, src, dst = _rec_inputs()

    def _L0_gnn_setup():
        import jax, jax.numpy as jnp
        import numpy as np
        N_NODES = 6250
        N_EDGES = 100000
        D = 64

        def _gin_layer(h, src, dst, W, b):
            agg = jax.ops.segment_sum(h[src], dst, num_segments=N_NODES)
            return (h + agg) @ W + b
        key = jax.random.key(seed)
        k_x, k_e, k_w1, k_w2 = jax.random.split(key, 4)
        node_emb = jax.random.normal(k_x, (N_NODES, D), dtype=jnp.float32)
        edge_index = jax.random.randint(k_e, (2, N_EDGES), 0, N_NODES, dtype=jnp.int64)
        s = 1.0 / np.sqrt(D)
        W1 = jax.random.normal(k_w1, (D, D), dtype=jnp.float32) * s
        b1 = jnp.zeros((D,), dtype=jnp.float32)
        W2 = jax.random.normal(k_w2, (D, D), dtype=jnp.float32) * s
        b2 = jnp.zeros((D,), dtype=jnp.float32)
        return {'node_emb': node_emb, 'edge_index': edge_index, 'W1': W1, 'b1': b1, 'W2': W2, 'b2': b2}
    _L0_gnn_all = _L0_gnn_setup()
    _L0_gnn_in = {k: v for k, v in _L0_gnn_all.items() if k in ('W1', 'b1', 'W2', 'b2')}
    del _L0_gnn_all

    def _L1_gnn_setup():
        import jax, jax.numpy as jnp
        import numpy as np
        N = 6250
        E = 100000
        C = 64
        H = 64
        EPS = 1e-05

        def _bn(h, gamma, beta):
            m = h.mean(axis=0)
            v = ((h - m) ** 2).mean(axis=0)
            return (h - m) * jax.lax.rsqrt(v + EPS) * gamma + beta
        key = jax.random.key(seed)
        ks = jax.random.split(key, 8)

        def glorot(k, shape):
            return jax.random.normal(k, shape, dtype=jnp.float32) / jnp.sqrt(jnp.float32(shape[0]))
        x = jax.random.normal(ks[0], (N, C), dtype=jnp.float32)
        edge_index = jax.random.randint(ks[1], (2, E), 0, N)
        return {'x': x, 'edge_index': edge_index, 'W_unite': glorot(ks[2], (2 * C, H)), 'b_unite': jnp.zeros((H,), jnp.float32), 'g1': jnp.ones((H,), jnp.float32), 'be1': jnp.zeros((H,), jnp.float32), 'W_gconv': glorot(ks[3], (2 * H, H)), 'b_gconv': jnp.zeros((H,), jnp.float32), 'g2': jnp.ones((H,), jnp.float32), 'be2': jnp.zeros((H,), jnp.float32), 'W_transfer': glorot(ks[4], (2 * H, H)), 'b_transfer': jnp.zeros((H,), jnp.float32), 'W_lin': glorot(ks[5], (H, H)), 'b_lin': jnp.zeros((H,), jnp.float32), 'g3': jnp.ones((H,), jnp.float32), 'be3': jnp.zeros((H,), jnp.float32)}
    _L1_gnn_all = _L1_gnn_setup()
    _L1_gnn_in = {k: v for k, v in _L1_gnn_all.items() if k in ('W_unite', 'b_unite', 'g1', 'be1', 'W_gconv', 'b_gconv', 'g2', 'be2', 'W_transfer', 'b_transfer', 'W_lin', 'b_lin', 'g3', 'be3')}
    del _L1_gnn_all
    return {'x': x, 'src': src, 'dst': dst, 'L0_gnn_W1': _L0_gnn_in['W1'], 'L0_gnn_b1': _L0_gnn_in['b1'], 'L0_gnn_W2': _L0_gnn_in['W2'], 'L0_gnn_b2': _L0_gnn_in['b2'], 'L1_gnn_W_unite': _L1_gnn_in['W_unite'], 'L1_gnn_b_unite': _L1_gnn_in['b_unite'], 'L1_gnn_g1': _L1_gnn_in['g1'], 'L1_gnn_be1': _L1_gnn_in['be1'], 'L1_gnn_W_gconv': _L1_gnn_in['W_gconv'], 'L1_gnn_b_gconv': _L1_gnn_in['b_gconv'], 'L1_gnn_g2': _L1_gnn_in['g2'], 'L1_gnn_be2': _L1_gnn_in['be2'], 'L1_gnn_W_transfer': _L1_gnn_in['W_transfer'], 'L1_gnn_b_transfer': _L1_gnn_in['b_transfer'], 'L1_gnn_W_lin': _L1_gnn_in['W_lin'], 'L1_gnn_b_lin': _L1_gnn_in['b_lin'], 'L1_gnn_g3': _L1_gnn_in['g3'], 'L1_gnn_be3': _L1_gnn_in['be3']}

def reference(x, src, dst, L0_gnn_W1, L0_gnn_b1, L0_gnn_W2, L0_gnn_b2, L1_gnn_W_unite, L1_gnn_b_unite, L1_gnn_g1, L1_gnn_be1, L1_gnn_W_gconv, L1_gnn_b_gconv, L1_gnn_g2, L1_gnn_be2, L1_gnn_W_transfer, L1_gnn_b_transfer, L1_gnn_W_lin, L1_gnn_b_lin, L1_gnn_g3, L1_gnn_be3):
    import jax
    import jax.numpy as jnp

    def _L0_gnn_ref(node_emb, edge_index, W1, b1, W2, b2):
        import jax, jax.numpy as jnp
        import numpy as np
        N_NODES = 6250
        N_EDGES = 100000
        D = 64

        def _gin_layer(h, src, dst, W, b):
            agg = jax.ops.segment_sum(h[src], dst, num_segments=N_NODES)
            return (h + agg) @ W + b
        src, dst = (edge_index[0], edge_index[1])
        h = _gin_layer(node_emb, src, dst, W1, b1)
        out = _gin_layer(h, src, dst, W2, b2)
        return out

    def _L1_gnn_ref(x, edge_index, W_unite, b_unite, g1, be1, W_gconv, b_gconv, g2, be2, W_transfer, b_transfer, W_lin, b_lin, g3, be3):
        import jax, jax.numpy as jnp
        import numpy as np
        N = 6250
        E = 100000
        C = 64
        H = 64
        EPS = 1e-05

        def _bn(h, gamma, beta):
            m = h.mean(axis=0)
            v = ((h - m) ** 2).mean(axis=0)
            return (h - m) * jax.lax.rsqrt(v + EPS) * gamma + beta
        n = x.shape[0]
        src_e = edge_index[0]
        dst_e = edge_index[1]
        self_idx = jnp.arange(n)
        rows_src = jnp.concatenate([self_idx, src_e])
        rows_dom = jnp.concatenate([self_idx, dst_e])
        f = x[rows_src]
        dsum = jax.ops.segment_sum(f, rows_dom, num_segments=n)
        h = jnp.concatenate([f, dsum[rows_dom]], axis=-1) @ W_unite + b_unite
        h = jax.nn.relu(_bn(h, g1, be1))
        s = jax.ops.segment_sum(h, rows_dom, num_segments=n)
        msg = jax.ops.segment_sum(s[src_e], dst_e, num_segments=n)
        h2 = jnp.concatenate([h, msg[rows_dom]], axis=-1) @ W_gconv + b_gconv
        h2 = jax.nn.relu(_bn(h2, g2, be2))
        agg = jax.ops.segment_sum(h2, rows_src, num_segments=n)
        t = jnp.concatenate([h2[:n], agg], axis=-1) @ W_transfer + b_transfer
        t = jax.nn.relu(_bn(t, g2, be2))
        out = jax.nn.relu(t @ W_lin + b_lin)
        out = jax.nn.relu(_bn(out, g3, be3))
        return out
    edge_index = jnp.stack([src, dst])
    x = _layernorm(x + _L0_gnn_ref(x, edge_index, L0_gnn_W1, L0_gnn_b1, L0_gnn_W2, L0_gnn_b2), axis=-1)
    x = _layernorm(x + _L1_gnn_ref(x, edge_index, L1_gnn_W_unite, L1_gnn_b_unite, L1_gnn_g1, L1_gnn_be1, L1_gnn_W_gconv, L1_gnn_b_gconv, L1_gnn_g2, L1_gnn_be2, L1_gnn_W_transfer, L1_gnn_b_transfer, L1_gnn_W_lin, L1_gnn_b_lin, L1_gnn_g3, L1_gnn_be3), axis=-1)
    return x

_drawn_inputs = setup_inputs


def setup_inputs(seed=0):
    import zlib

    import numpy as np

    out = dict(_drawn_inputs(seed))
    spreads = {'L0_gnn_b1': (0.0, 0.1),
     'L0_gnn_b2': (0.0, 0.1),
     'L1_gnn_b_unite': (0.0, 0.1),
     'L1_gnn_g1': (1.0, 0.2),
     'L1_gnn_be1': (0.0, 0.1),
     'L1_gnn_b_gconv': (0.0, 0.1),
     'L1_gnn_g2': (1.0, 0.2),
     'L1_gnn_be2': (0.0, 0.1),
     'L1_gnn_b_transfer': (0.0, 0.1),
     'L1_gnn_b_lin': (0.0, 0.1),
     'L1_gnn_g3': (1.0, 0.2),
     'L1_gnn_be3': (0.0, 0.1)}
    factors = {}
    for name, (base, spread) in spreads.items():
        noise = np.random.default_rng([zlib.crc32(name.encode()), seed]).standard_normal(out[name].shape)
        drawn = base * np.exp(spread * noise) if base else spread * noise
        out[name] = jnp.asarray(drawn.astype(out[name].dtype))
    for name, factor in factors.items():
        out[name] = (out[name] * factor).astype(out[name].dtype)
    return out
```

```python
from contextlib import ExitStack

import concourse.bass as bass
from concourse import mybir

F32 = mybir.dt.float32
I32 = mybir.dt.int32
BF16 = mybir.dt.bfloat16
ALU = mybir.AluOpType
ACT = mybir.ActivationFunctionType
ENG = mybir.EngineType
AX = mybir.AxisListType.X

P = 128
N = 6250
E = 200000
D = 64
T = -(-N // P)
LAST = N - (T - 1) * P
C = -(-E // P)
FULL = E // P
G = 8
ITER = -(-(C + T - 1) // (2 * G))
KB = -(-ITER * 2 * G // P)
K = KB * P
NO_NODE = 8191
TRASH = T * P
TAB = (T + 1) * P
EPS = 1e-5
ROWS = N + E
LT = 7
NG = T // LT
VECS = ["L0_b1", "L0_b2", "b_unite", "g1", "be1", "b_gconv", "g2", "be2", "b_transfer", "b_lin", "g3", "be3"]
VEC = {name: i for i, name in enumerate(VECS)}
MATS = ["L0_W1", "L0_W2", "WuP", "WuV", "WgH", "WgU", "W_lin"]
MAT = {name: i for i, name in enumerate(MATS)}


def build(nc, x, src, dst, mats, vecs, w_transfer, out):
    with ExitStack() as ctx:
        def sb(name, shape, dt=F32):
            return ctx.enter_context(nc.sbuf_tensor(name, shape, dt))

        def sem(name):
            return ctx.enter_context(nc.semaphore(name))

        def dram(name, shape, dt=F32):
            return nc.dram_tensor(name, shape, dt, kind="Internal").ap()

        edges = dram("edges", (C, 2 * P), I32)
        tile_of_step = dram("tile_of_step", (K,), I32)
        hid_rows = dram("hid_rows", (TRASH, D))
        pv_rows = dram("pv_rows", (TRASH, 3 * D))
        s_rows = dram("s_rows", (TRASH, D))
        p_rows = dram("p_rows", (TRASH, D))
        h_saved = dram("h_saved", (2 * ITER, P, G * D))
        tables = [dram(f"scatter{j}", (TAB, D)) for j in range(G)]

        ident = sb("ident", [P, P])
        ones = sb("ones", [P, P])
        tri = sb("tri", [P, P])
        iota_i = sb("iota_i", [P, P], I32)
        iota = sb("iota", [P, P])
        kcol_i = sb("kcol_i", [P, KB], I32)
        kcol = sb("kcol", [P, KB])
        trash = sb("trash", [P, 1])
        valid = sb("valid", [P, 1])
        vec_row = sb("vec_row", [1, len(VECS) * D])
        vec = sb("vec", [P, len(VECS), D])
        mat = sb("mat", [D, len(MATS), D])
        wtr = sb("wtr", [2 * D, D])
        pad = sb("pad", [1, 2, P], I32)
        ck = sb("ck", [P, KB])
        ck_i = sb("ck_i", [P, KB], I32)
        dk = sb("dk", [P, KB])
        dk_i = sb("dk_i", [P, KB], I32)
        dtab = sb("dtab", [1, K], I32)
        src_i = sb("src_i", [P, K], I32)
        dloc = sb("dloc", [P, K])
        srcm = sb("srcm", [P, K])
        mask = sb("mask", [P, K])
        X = sb("X", [P, T, D])
        X1 = sb("X1", [P, T, D])
        acc = sb("acc", [P, T, 3 * D])
        B1 = sb("B1", [P, T, D])
        B2 = sb("B2", [P, T, D])
        B3 = sb("B3", [P, T, D])
        B4 = sb("B4", [P, T, D])
        wdeg = sb("wdeg", [P, T])
        node = sb("node", [P, T, 2])
        oh = sb("oh", [P, 2, G, P])
        ident_b = sb("ident_b", [P, P], BF16)
        src_split = sb("src_split", [P, 2, K], BF16)
        src_b = sb("src_b", [P, 2, 2, G], BF16)
        ohT = sb("ohT", [P, 2, G, P])
        rows = sb("rows", [P, 2, G, 3 * D])
        idx = sb("idx", [P, 2, G], I32)
        work = sb("work", [P, 2, G, D])
        hm = sb("hm", [P, 2, G, D])
        dup = sb("dup", [P, 2, G])
        idx_f = sb("idx_f", [P, 2, G])
        xT = sb("xT", [P, LT * P])
        part = sb("part", [P, 5, D])
        nrm = sb("nrm", [P, 12, D])
        w2 = sb("w2", [D, D])
        gram = sb("gram", [D, D])
        gw = sb("gw", [D, D])
        oh_b = oh[:, 0].rearrange("p g d -> p (g d)").bitcast(BF16).rearrange("p (h g d) -> p h g d", h=2, g=G)
        rows_flat = rows[:].rearrange("p h g f -> p (h g f)")
        hT = rows_flat[0:D, 0:2 * G * P].rearrange("p (h c) -> p h c", h=2)
        hd = rows_flat[:, 2 * G * P:2 * G * P + 2 * G * D].rearrange("p (h g f) -> p h g f", h=2, g=G)
        acc_flat = acc[:].rearrange("p t f -> p (t f)")
        eq = acc_flat[:, 0:2 * G * P].rearrange("p (h g e) -> p h g e", h=2, g=G)
        before = acc_flat[:, 2 * G * P:3 * G * P].rearrange("p (g e) -> p g e", g=G)
        flat = [a[:].rearrange("p t f -> p (t f)") for a in (acc, B1, B2, B3)]
        G_f = flat[0][:, 0:KB * 2 * P].rearrange("p (b e) -> p b e", e=2 * P)
        G_i = flat[0][:, KB * 2 * P:2 * KB * 2 * P].bitcast(I32).rearrange("p (b e) -> p b e", e=2 * P)
        last_i = flat[1][0:1, 0:C - 1].bitcast(I32)
        last_f = flat[1][0:1, C - 1:2 * (C - 1)]
        cnum_i = flat[2][0:1, 0:C - 1].bitcast(I32)
        cnum = flat[2][0:1, C - 1:2 * (C - 1)]
        ck_junk = flat[3][:, 0:C - 1]
        PS = ctx.enter_context(nc.psum_tensor("PS", [P, 8, 512], F32))

        def bank(b, n=1):
            return PS[:, b:b + n, :].rearrange("p b c -> p (b c)")

        s_const = sem("s_const")
        s_in = sem("s_in")
        s_x = sem("s_x")
        s_settle = sem("s_settle")
        s_made = sem("s_made")
        s_dve = sem("s_dve")
        s_sync = sem("s_sync")
        s_bcast = sem("s_bcast")
        s_vrow = sem("s_vrow")
        s_tr = sem("s_tr")
        cs_in, cs_out = sem("cs_in"), sem("cs_out")
        sq_in, sq_out = sem("sq_in"), sem("sq_out")
        s_gw = sem("s_gw")
        s_gram = sem("s_gram")
        s_dma = sem("s_dma")
        s_chunks = sem("s_chunks")
        primed = []

        def primed_sem(name):
            primed.append(sem(name))
            return primed[-1]

        def pair(name):
            return [primed_sem(f"{name}0"), primed_sem(f"{name}1")]

        def dma_pair(name):
            return [sem(f"{name}0"), sem(f"{name}1")]

        ln_ps, ln_cp, ln_mm, ln_out = [primed_sem(n) for n in ("ln_ps", "ln_cp", "ln_mm", "ln_out")]

        class Pass:
            def __init__(self, name):
                self.rows_in = dma_pair(f"{name}_rows_in")
                self.oh = pair(f"{name}_oh")
                self.segsum = pair(f"{name}_segsum")
                self.idx = sem(f"{name}_idx")
                self.added = primed_sem(f"{name}_added")

        passes = {n: Pass(n) for n in ["agg1", "agg2", "pv", "msg"]}
        e1_saved = dma_pair("e1_saved")
        e1_in, e1_used = dma_pair("e1_in"), pair("e1_used")
        e1_oh, e1_T, e1_ohT = pair("e1_oh"), pair("e1_T"), pair("e1_ohT")
        e1_q, e1_hm, e1_seg = pair("e1_q"), pair("e1_hm"), pair("e1_seg")
        e1_idx, e1_chain, e1_added = sem("e1_idx"), sem("e1_chain"), primed_sem("e1_added")
        e2_in = dma_pair("e2_in")
        e2_oh, e2_T, e2_ohT = pair("e2_oh"), pair("e2_T"), pair("e2_ohT")
        e2_pre, e2_hT, e2_z, e2_h2 = pair("e2_pre"), pair("e2_hT"), pair("e2_z"), pair("e2_h2")
        e2_src, e2_row, e2_eq, e2_sum, e2_hd = pair("e2_src"), pair("e2_row"), pair("e2_eq"), pair("e2_sum"), pair("e2_hd")
        e2_ixf, e2_idx, e2_chain = pair("e2_ixf"), pair("e2_idx"), sem("e2_chain")
        scattered = [sem(f"scattered{j}") for j in range(G)]
        tab_in = dma_pair("tab_in")

        block = ctx.enter_context(nc.Block())

        POINTS = (["pad", "vec", "vsteps", "ck", "dk", "chunks", "agg1", "h_in", "hid", "agg2", "out0_in", "x1",
                   "pv_rows", "pv", "edges1", "s", "HW_in", "msg", "U_in", "gram", "edges2"]
                  + [f"table{j}" for j in range(G)] + ["t_in", "lin_in", "out"])

        def at(engine, name):
            engine.wait_ge(s_sync, POINTS.index(name) + 1)

        def done(engine, s, i, h):
            engine.wait_ge(s[h], i + 2)

        def reuse(engine, s, i, h):
            engine.wait_ge(s[h], i + 1)

        def prior(engine, s, i, h):
            engine.wait_ge(s[1 - h], i + (h + 1))

        def load_tiles(which, i):
            return nc.values_load_multi_w_load_instructions(
                dtab[0:1, bass.ds(i * 2 * G, 2 * G)], engines=(which,), min_val=0, max_val=T - 1,
                skip_runtime_bounds_check_because="DVE has bounded the tiles of all steps")[1]

        def settle(pool):
            pool.sem_inc(s_settle, 1)

        def seg_bank(h, j, width):
            return bank(4 * h, 4)[:, 256 * j:256 * j + width]

        def pool_gather(pool, name, table, width):
            p = passes[name]
            with pool.Fori(0, ITER) as i:
                for h in range(2):
                    reuse(pool, p.segsum, i, h)
                    settle(pool)
                    nc.gpsimd.tensor_copy(idx[:, h, :], src_i[:, bass.ds(i * 2 * G + h * G, G)]).then_inc(p.idx, 1)
                    pool.wait_ge(p.idx, i * 2 + h + 1)
                    settle(pool)
                    for j in range(G):
                        pool.indirect_dma_start(
                            out=rows[:, h, j, 0:width], out_offset=None, in_=table,
                            in_offset=bass.IndirectOffsetOnAxis(ap=idx[:, h, j:j + 1], axis=0),
                        ).then_inc(p.rows_in[h], 16)

        def pe_segsum(pe, name, width):
            p = passes[name]
            with pe.Fori(0, ITER) as i:
                for h in range(2):
                    pe.wait_ge(p.rows_in[h], i * 16 * G + 16 * G)
                    done(pe, p.oh, i, h)
                    pe.wait_ge(p.added, i * 2 * G + 1)
                    for j in range(G):
                        last = nc.tensor.matmul(seg_bank(h, j, width), oh[:, h, j, :], rows[:, h, j, 0:width],
                                                start=True, stop=True)
                    last.then_inc(p.segsum[h], 1)

        def one_hots(i, h, to=oh):
            return nc.vector.tensor_tensor(
                to[:, h], iota[:].unsqueeze(1).to_broadcast([P, G, P]),
                dloc[:, bass.ds(i * 2 * G + h * G, G)].unsqueeze(2).to_broadcast([P, G, P]), ALU.is_equal)

        def add_steps(dve, i, h, tiles, added, sums, width):
            for j in range(G):
                a = acc[:, bass.ds(tiles[h * G + j], 1), 0:width].rearrange("p a f -> p (a f)")
                dve.wait_ge(added, i * 2 * G + (h * G + j + 1))
                nc.vector.tensor_tensor(a, a, sums(j), ALU.add).then_inc(added, 1)

        def dve_segsum(dve, name, width):
            p = passes[name]
            with dve.Fori(0, ITER) as i:
                tiles = load_tiles(ENG.DVE, i)
                for h in range(2):
                    reuse(dve, p.segsum, i, h)
                    one_hots(i, h).then_inc(p.oh[h], 1)
                for h in range(2):
                    done(dve, p.segsum, i, h)
                    add_steps(dve, i, h, tiles, p.added, lambda j: seg_bank(h, j, width), width)
            dve.wait_ge(p.added, ITER * 2 * G + 1)

        LINEAR = ["h", "out0", "pv", "SW", "HW", "U", "t", "lin"]

        def pe_linear(pe, name, inp, kin, w, nout):
            s = NG * LINEAR.index(name)
            for t in range(NG):
                pe.wait_ge(ln_cp, t + s + 1)
                for j in range(LT):
                    last = nc.tensor.matmul(bank(0, 2)[0:kin, P * j:P * j + P], inp[:, t * LT + j, :],
                                            ident[:], start=True, stop=True)
                last.then_inc(ln_ps, 1)
                pe.wait_ge(ln_cp, t + (s + 2))
                pe.wait_ge(ln_out, t + s + 1)
                for j in range(LT):
                    last = nc.tensor.matmul(bank(2, 2)[:, P * j:P * j + nout], xT[0:kin, P * j:P * j + P], w,
                                            start=True, stop=True)
                last.then_inc(ln_mm, 1)

        def act_linear(act, name, kin):
            s = NG * LINEAR.index(name)
            with act.Fori(0, NG) as t:
                act.wait_ge(ln_ps, t + (s + 2))
                act.wait_ge(ln_mm, t + (s + 1))
                nc.scalar.copy(xT[0:kin, :], bank(0, 2)[0:kin, 0:LT * P]).then_inc(ln_cp, 1)

        def dve_linear(dve, name, outs):
            s = NG * LINEAR.index(name)
            with dve.Fori(0, NG) as t:
                dve.wait_ge(ln_mm, t + (s + 2))
                for n, (o, col, bias) in enumerate(outs):
                    ps = bank(2, 2)[:, 0:LT * P].rearrange("p (j c) -> p j c", c=P)[:, :, col:col + D]
                    to = o[:, bass.ds(t * LT, LT), :]
                    if bias is None:
                        last = nc.vector.tensor_copy(to, ps)
                    else:
                        b = vec[:, VECS.index(bias), :].unsqueeze(1).to_broadcast([P, LT, D])
                        last = nc.vector.tensor_tensor(to, ps, b, ALU.add)
                last.then_inc(ln_out, 1)
            dve.wait_ge(ln_out, s + NG + 1)

        def M(name):
            return mat[:, MATS.index(name), :]

        N_IN = 16 * (3 + 2 * (E % P > 0) + 2 * (E % P > 0))
        NX = 16 * 5
        moved = [0]

        @block.sync
        def _(sp):
            sp.dma_start(vec_row[:], vecs).then_inc(s_x, 16)
            sp.dma_start(mat[:], mats.rearrange("m k n -> k m n")).then_inc(s_x, 16)
            sp.dma_start(wtr[:], w_transfer).then_inc(s_x, 16)
            sp.dma_start(X[:, 0:T - 1, :], x[0:(T - 1) * P, :].rearrange("(t p) f -> p t f", p=P)).then_inc(s_x, 16)
            lasts = dst[0:(C - 1) * P].rearrange("(c e) -> e c", e=P)[P - 1:P, :]
            sp.dma_start(last_i, lasts, allow_slow_non_contiguous=True).then_inc(s_in, 16)
            sp.dma_start(edges[0:FULL, 0:P], src[0:FULL * P].rearrange("(c e) -> c e", e=P)).then_inc(s_in, 16)
            sp.dma_start(edges[0:FULL, P:2 * P], dst[0:FULL * P].rearrange("(c e) -> c e", e=P)).then_inc(s_in, 16)
            sp.dma_start(edges[FULL:C, 0:E % P], src[FULL * P:E].unsqueeze(0)).then_inc(s_in, 16)
            sp.dma_start(edges[FULL:C, P:P + E % P], dst[FULL * P:E].unsqueeze(0)).then_inc(s_in, 16)
            at(sp, "pad")
            sp.dma_start(X[0:LAST, T - 1, :], x[(T - 1) * P:N, :]).then_inc(s_x, 16)
            sp.dma_start(edges[FULL:C, E % P:P], pad[0:1, 0, E % P:P]).then_inc(s_in, 16)
            sp.dma_start(edges[FULL:C, P + E % P:2 * P], pad[0:1, 1, E % P:P]).then_inc(s_in, 16)

            def move(to, of, **how):
                moved[0] += 16
                sp.dma_start(to, of, **how).then_inc(s_dma, 16)
                sp.wait_ge(s_dma, moved[0])

            at(sp, "dk")
            move(tile_of_step.rearrange("(b p) -> p b", p=P), dk_i[:], allow_slow_non_contiguous=True)
            move(dtab[0:1, :], tile_of_step.unsqueeze(0))
            at(sp, "hid")
            move(hid_rows.rearrange("(t p) f -> p t f", p=P), B2[:])
            at(sp, "pv_rows")
            move(pv_rows.rearrange("(t p) f -> p t f", p=P), acc[:])
            move(p_rows.rearrange("(t p) f -> p t f", p=P), B1[:])
            at(sp, "edges1")
            for h in range(2):
                sp.dma_start(h_saved[h, 0:1, 0:D], X1[0:1, 0, :]).then_inc(e1_saved[h], 16)
            for h in range(2):
                sp.wait_ge(e1_saved[h], 16)
            with sp.Fori(0, ITER) as i:
                for h in range(2):
                    done(sp, e1_hm, i, h)
                    sp.dma_start(h_saved[bass.ds(i * 2 + h, 1)].rearrange("a p c -> p (a c)"),
                                 hm[:, h].rearrange("p g f -> p (g f)")).then_inc(e1_saved[h], 16)
            at(sp, "s")
            move(s_rows.rearrange("(t p) f -> p t f", p=P), B1[:])
            for h in range(2):
                sp.wait_ge(e1_saved[h], ITER * 16 + 16)
            with sp.Fori(0, ITER) as i:
                for h in range(2):
                    reuse(sp, e2_pre, i, h)
                    sp.dma_start(work[:, h].rearrange("p g f -> p (g f)"),
                                 h_saved[bass.ds(i * 2 + h, 1)].rearrange("a p c -> p (a c)")).then_inc(e2_in[h], 16)
            for j in range(G):
                sp.wait_ge(scattered[j], 16 * 2 * ITER + 32)
                if j >= 2:
                    at(sp, f"table{j - 2}")
                sp.dma_start([B1, B3][j % 2][:], tables[j][0:TRASH, :].rearrange("(t p) f -> p t f", p=P)
                             ).then_inc(tab_in[j % 2], 16)
            at(sp, "out")
            move(out[0:(T - 1) * P, :].rearrange("(t p) f -> p t f", p=P), B1[:, 0:T - 1, :])
            move(out[(T - 1) * P:N, :], B1[0:LAST, T - 1, :])

        @block.gpsimd
        def _(pool):
            made = [0]

            def make(ins):
                made[0] += 1
                ins.then_inc(s_made, 1)
                pool.wait_ge(s_made, made[0])

            make(nc.gpsimd.memset(ones[:], 1.0))
            make(nc.gpsimd.affine_select(out=ident[:], in_=ones[:], compare_op=ALU.is_equal, fill=0.0, base=0,
                                         pattern=[[-1, P]], channel_multiplier=1))
            make(nc.gpsimd.affine_select(out=tri[:], in_=ones[:], compare_op=ALU.is_gt, fill=0.0, base=0,
                                         pattern=[[-1, P]], channel_multiplier=1))
            make(nc.gpsimd.affine_select(out=valid[:], in_=ones[:, 0:1], compare_op=ALU.is_gt, fill=0.0, base=LAST,
                                         pattern=[[0, 1]], channel_multiplier=-1))
            make(nc.gpsimd.iota(iota_i[:], pattern=[[1, P]], base=0, channel_multiplier=0))
            make(nc.gpsimd.iota(kcol_i[:], pattern=[[P, KB]], base=0, channel_multiplier=1))
            make(nc.gpsimd.iota(cnum_i[:], pattern=[[1, C - 1]], base=1, channel_multiplier=0))
            make(nc.gpsimd.tensor_copy(iota[:], iota_i[:]))
            make(nc.gpsimd.tensor_copy(kcol[:], kcol_i[:]))
            make(nc.gpsimd.tensor_copy(cnum[:], cnum_i[:]))
            make(nc.gpsimd.tensor_scalar(trash[:], kcol[:, 0:1], float(TRASH), None, ALU.add))
            make(nc.gpsimd.memset(rows[:], 1.0))
            for s in primed:
                pool.sem_inc(s, 1)
            at(pool, "pad")
            for j in range(G):
                pool.dma_start(tables[j][0:TRASH, :].rearrange("(t p) f -> p t f", p=P), B4[:]).then_inc(scattered[j], 16)
                pool.dma_start(tables[j][TRASH:TAB, :], B4[:, 0, :]).then_inc(scattered[j], 16)
            pool.sem_inc(s_const, 1)

            at(pool, "ck")
            pool.wait_ge(s_in, N_IN)
            for b in range(KB):
                pool.indirect_dma_start(out=G_i[:, b, :], out_offset=None, in_=edges,
                                        in_offset=bass.IndirectOffsetOnAxis(ap=ck_i[:, b:b + 1], axis=0),
                                        ).then_inc(s_chunks, 16)
            at(pool, "agg1")
            pool_gather(pool, "agg1", x, D)
            at(pool, "agg2")
            pool.wait_ge(s_dma, 48)
            pool_gather(pool, "agg2", hid_rows, D)
            at(pool, "pv")
            pool_gather(pool, "pv", pv_rows, 3 * D)
            at(pool, "edges1")
            pool.wait_ge(s_dma, 80)
            with pool.Fori(0, ITER) as i:
                for h in range(2):
                    reuse(pool, e1_used, i, h)
                    settle(pool)
                    nc.gpsimd.tensor_copy(idx[:, h, :], src_i[:, bass.ds(i * 2 * G + h * G, G)]).then_inc(e1_idx, 1)
                    pool.wait_ge(e1_idx, i * 2 + h + 1)
                    settle(pool)
                    for j in range(G):
                        pool.indirect_dma_start(
                            out=work[:, h, j, :], out_offset=None, in_=p_rows,
                            in_offset=bass.IndirectOffsetOnAxis(ap=idx[:, h, j:j + 1], axis=0),
                        ).then_inc(e1_in[h], 16)
            at(pool, "msg")
            pool.wait_ge(s_dma, 96)
            pool_gather(pool, "msg", s_rows, D)
            with pool.Fori(0, ITER) as i:
                for h in range(2):
                    done(pool, e2_ixf, i, h)
                    settle(pool)
                    nc.gpsimd.tensor_copy(idx[:, h, :], idx_f[:, h, :]).then_inc(e2_idx[h], 1)
                    done(pool, e2_idx, i, h)
                    done(pool, e2_hd, i, h)
                    for j in range(G):
                        pool.wait_ge(scattered[j], i * 32 + (16 * h + 32))
                        settle(pool)
                        pool.indirect_dma_start(
                            out=tables[j], out_offset=bass.IndirectOffsetOnAxis(ap=idx[:, h, j:j + 1], axis=0),
                            in_=hd[:, h, j, :], in_offset=None, compute_op=ALU.add).then_inc(scattered[j], 16)

        sums = [0]

        @block.tensor
        def _(pe):
            pe.wait_ge(s_const, 1)
            pe.wait_ge(s_x, NX)
            nv = len(VECS) * D
            for b in range(0, nv, 512):
                w = min(512, nv - b)
                last = nc.tensor.matmul(bank(0, 2)[:, b:b + w], ones[0:1, :], vec_row[0:1, b:b + w], start=True, stop=True)
            last.then_inc(s_bcast, 1)
            at(pe, "vsteps")
            for b in range(0, C - 1, 512):
                w = min(512, C - 1 - b)
                last = nc.tensor.matmul(bank(2, 4)[:, b:b + w], ones[0:1, :], last_f[0:1, b:b + w], start=True, stop=True)
            last.then_inc(s_vrow, 1)
            at(pe, "chunks")
            for half in range(2):
                for b in range(KB):
                    last = nc.tensor.matmul(bank(4 * half, 4)[:, P * b:P * b + P], G_f[:, b, P * half:P * half + P],
                                            ident[:], start=True, stop=True)
            last.then_inc(s_tr, 1)

            def sum_nodes(n):
                sums[0] += 1
                pe.wait_ge(cs_in, sums[0])
                nc.tensor.matmul(bank(4)[:, 0:n * D], ones[:], part[:, 0:n, :].rearrange("p n f -> p (n f)"),
                                 start=True, stop=True).then_inc(cs_out, 1)

            at(pe, "agg1")
            pe_segsum(pe, "agg1", D + 1)
            at(pe, "h_in")
            pe_linear(pe, "h", B1, D, M("L0_W1"), D)
            at(pe, "agg2")
            pe_segsum(pe, "agg2", D)
            at(pe, "out0_in")
            pe_linear(pe, "out0", B1, D, M("L0_W2"), D)
            at(pe, "x1")
            pe_linear(pe, "pv", X1, D, mat[:, MATS.index("WuP"):MATS.index("WuV") + 1, :].rearrange("k m n -> k (m n)"), 2 * D)
            sum_nodes(1)
            at(pe, "pv")
            pe_segsum(pe, "pv", 3 * D)
            sum_nodes(1)
            sum_nodes(5)
            at(pe, "edges1")
            nc.tensor.matmul(bank(6)[0:D, 0:D], B4[:, 0, :], B4[:, 0, :], start=True, stop=False, skip_group_check=True)
            for t in range(1, T):
                nc.tensor.matmul(bank(6)[0:D, 0:D], B4[:, t, :], B4[:, t, :], start=False, stop=False, skip_group_check=True)
            with pe.Fori(0, ITER) as i:
                tiles = load_tiles(ENG.PE, i)
                for h in range(2):
                    done(pe, e1_oh, i, h)
                    reuse(pe, e1_ohT, i, h)
                    for j in range(G):
                        last = nc.tensor.matmul(bank(2 * h, 2)[:, P * j:P * j + P], oh[:, h, j, :], ident[:],
                                                start=True, stop=True)
                    last.then_inc(e1_T[h], 1)
                for h in range(2):
                    done(pe, e1_ohT, i, h)
                    pe.wait_ge(e1_added, i * 2 * G + 1)
                    for j in range(G):
                        last = nc.tensor.matmul(bank(4 + h)[:, D * j:D * j + D], ohT[:, h, j, :],
                                                B3[:, bass.ds(tiles[h * G + j], 1), :].rearrange("p a f -> p (a f)"),
                                                start=True, stop=True)
                    last.then_inc(e1_q[h], 1)
                for h in range(2):
                    done(pe, e1_hm, i, h)
                    for j in range(G):
                        nc.tensor.matmul(bank(6)[0:D, 0:D], hm[:, h, j, :], hm[:, h, j, :], start=False, stop=False,
                                         skip_group_check=True)
                    for j in range(G):
                        last = nc.tensor.matmul(bank(4 + h)[:, D * j:D * j + D], oh[:, h, j, :], hm[:, h, j, :],
                                                start=True, stop=True)
                    last.then_inc(e1_seg[h], 1)
            at(pe, "s")
            pe_linear(pe, "SW", B1, D, M("WgH"), D)
            pe_linear(pe, "HW", B4, D, M("WgH"), D)
            at(pe, "msg")
            pe.wait_ge(s_gram, 1)
            pe_segsum(pe, "msg", D)
            at(pe, "U_in")
            pe_linear(pe, "U", B1, D, M("WgU"), D)
            sum_nodes(1)
            nc.tensor.matmul(bank(5)[0:D, 0:D], gram[:], M("WgH"), start=True, stop=True).then_inc(s_gw, 1)
            sum_nodes(5)

            at(pe, "edges2")

            def rows_and_transposes(i, h):
                done(pe, e2_src, i, h)
                prior(pe, e2_eq, i, h)
                for j in range(G):
                    for part_of in range(2):
                        last = nc.tensor.matmul(bank(5, 2)[:, P * j:P * j + P],
                                                src_b[:, h, part_of, j:j + 1].to_broadcast([P, P]), ident_b[:],
                                                start=part_of == 0, stop=part_of == 1)
                last.then_inc(e2_row[h], 1)
                done(pe, e2_oh, i, h)
                prior(pe, e2_ohT, i, h)
                for j in range(G):
                    last = nc.tensor.matmul(bank(0, 2)[:, P * j:P * j + P], oh_b[:, h, j, :], ident_b[:],
                                            start=True, stop=True)
                last.then_inc(e2_T[h], 1)

            def by_feature(i, h):
                pe.wait_ge(e2_in[h], i * 16 + 16)
                prior(pe, e2_hT, i, h)
                for j in range(G):
                    last = nc.tensor.matmul(bank(2, 2)[0:D, P * j:P * j + P], work[:, h, j, :], ident[:],
                                            start=True, stop=True)
                last.then_inc(e2_pre[h], 1)

            def second(i, h, tiles):
                done(pe, e2_hT, i, h)
                done(pe, e2_ohT, i, h)
                prior(pe, e2_h2, i, h)
                for j in range(G):
                    to = bank(4)[:, D * j:D * j + D]
                    nc.tensor.matmul(to, hT[:, h, P * j:P * j + P], w2[:], start=True, stop=False)
                    last = nc.tensor.matmul(to, ohT[:, h, j, :], B4[:, bass.ds(tiles[h * G + j], 1), :].rearrange("p a f -> p (a f)"),
                                            start=False, stop=True)
                last.then_inc(e2_z[h], 1)

            def by_source(i, h):
                done(pe, e2_h2, i, h)
                done(pe, e2_eq, i, h)
                prior(pe, e2_hd, i, h)
                for j in range(G):
                    last = nc.tensor.matmul(bank(7)[:, D * j:D * j + D], eq[:, h, j, :], hm[:, h, j, :],
                                            start=True, stop=True)
                last.then_inc(e2_sum[h], 1)

            with pe.Fori(0, ITER) as i:
                tiles = load_tiles(ENG.PE, i)
                rows_and_transposes(i, 0)
                by_feature(i, 0)
                rows_and_transposes(i, 1)
                second(i, 0, tiles)
                by_feature(i, 1)
                by_source(i, 0)
                second(i, 1, tiles)
                by_source(i, 1)
            at(pe, "t_in")
            pe_linear(pe, "t", acc[:, :, 0:2 * D], 2 * D, wtr[:], D)
            sum_nodes(1)
            sum_nodes(1)
            at(pe, "lin_in")
            pe_linear(pe, "lin", B1, D, M("W_lin"), D)
            sum_nodes(1)
            sum_nodes(1)

        roots = [0]

        @block.scalar
        def _(act):
            def root(ap):
                roots[0] += 1
                act.wait_ge(sq_in, roots[0])
                nc.scalar.activation(ap, ap, ACT.Sqrt).then_inc(sq_out, 1)

            act_linear(act, "h", D)
            act_linear(act, "out0", D)
            root(node[:, :, 1])
            act_linear(act, "pv", D)
            root(nrm[:, 0, :])
            with act.Fori(0, ITER) as i:
                for h in range(2):
                    done(act, e1_T, i, h)
                    reuse(act, e1_q, i, h)
                    nc.scalar.copy(ohT[:, h].rearrange("p g e -> p (g e)"), bank(2 * h, 2)).then_inc(e1_ohT[h], 1)
            act_linear(act, "SW", D)
            act_linear(act, "HW", D)
            act_linear(act, "U", D)
            root(nrm[:, 2, :])
            at(act, "edges2")

            def copy_transposes(i, h):
                done(act, e2_T, i, h)
                reuse(act, e2_z, i, h)
                nc.scalar.copy(ohT[:, h].rearrange("p g e -> p (g e)"), bank(0, 2)).then_inc(e2_ohT[h], 1)

            def copy_by_feature(i, h):
                done(act, e2_pre, i, h)
                reuse(act, e2_z, i, h)
                nc.scalar.copy(hT[:, h, :], bank(2, 2)[0:D, :]).then_inc(e2_hT[h], 1)

            def second_relu(i, h):
                done(act, e2_z, i, h)
                reuse(act, e2_sum, i, h)
                nc.scalar.activation(hm[:, h].rearrange("p g f -> p (g f)"), bank(4), ACT.Relu).then_inc(e2_h2[h], 1)

            def copy_sums(i, h):
                done(act, e2_sum, i, h)
                for j in range(G):
                    act.wait_ge(scattered[j], i * 32 + (16 * h + 16))
                nc.scalar.copy(hd[:, h].rearrange("p g f -> p (g f)"), bank(7)).then_inc(e2_hd[h], 1)

            with act.Fori(0, ITER) as i:
                copy_transposes(i, 0)
                copy_by_feature(i, 0)
                copy_transposes(i, 1)
                second_relu(i, 0)
                copy_by_feature(i, 1)
                copy_sums(i, 0)
                second_relu(i, 1)
                copy_sums(i, 1)
            act_linear(act, "t", 2 * D)
            root(nrm[:, 0, :])
            act_linear(act, "lin", D)
            root(nrm[:, 0, :])
            root(node[:, :, 1])

        @block.vector
        def _(dve):
            steps, points, asked, rooted = [0], [0], [0], [0]
            v = nc.vector

            def step(ins):
                steps[0] += 1
                ins.then_inc(s_dve, 1)
                dve.wait_ge(s_dve, steps[0])

            def reach(name):
                assert POINTS[points[0]] == name, (POINTS[points[0]], name)
                points[0] += 1
                dve.sem_inc(s_sync, 1)

            def tt(o, a, b, op):
                step(v.tensor_tensor(o, a, b, op))

            def ts(o, a, s1, s2, op0, op1=None):
                step(v.tensor_scalar(o, a, s1, s2, op0) if op1 is None else v.tensor_scalar(o, a, s1, s2, op0, op1))

            def wide(row):
                return row.unsqueeze(1).to_broadcast([P, T, D])

            def deg(a):
                return a.unsqueeze(2).to_broadcast([P, T, D])

            def clear_tail(a):
                ts(a[:, T - 1, :], a[:, T - 1, :], valid[:, 0:1], None, ALU.mult)

            def fold(slot, a):
                step(v.tensor_reduce(part[:, slot, :], a.rearrange("p t f -> p f t"), AX, ALU.add))

            def ask_sums():
                asked[0] += 1
                dve.sem_inc(cs_in, 1)
                dve.wait_ge(cs_out, asked[0])

            def ask_root():
                rooted[0] += 1
                dve.sem_inc(sq_in, 1)
                dve.wait_ge(sq_out, rooted[0])

            def total(n):
                return bank(4)[:, n * D:n * D + D]

            def center(a, count):
                clear_tail(a)
                fold(0, a)
                ask_sums()
                ts(nrm[:, 8, :], total(0), 1.0 / count, None, ALU.mult)
                tt(a, a, wide(nrm[:, 8, :]), ALU.subtract)
                clear_tail(a)

            def scale_of(var, gamma, to):
                ts(var, var, EPS, None, ALU.add)
                ask_root()
                step(v.reciprocal(var, var))
                tt(to, var, vec[:, VECS.index(gamma), :], ALU.mult)

            def node_norm(a, gamma, beta, tmp):
                center(a, N)
                tt(tmp, a, a, ALU.mult)
                fold(0, tmp)
                ask_sums()
                ts(nrm[:, 0, :], total(0), 1.0 / N, None, ALU.mult)
                scale_of(nrm[:, 0, :], gamma, nrm[:, 0, :])
                tt(a, a, wide(nrm[:, 0, :]), ALU.mult)
                tt(a, a, wide(vec[:, VECS.index(beta), :]), ALU.add)
                ts(a, a, 0.0, None, ALU.max)
                clear_tail(a)

            def layer_norm(o, a, tmp):
                step(v.tensor_reduce(node[:, :, 0], a, AX, ALU.add))
                ts(node[:, :, 0], node[:, :, 0], 1.0 / D, None, ALU.mult)
                tt(a, a, deg(node[:, :, 0]), ALU.subtract)
                tt(tmp, a, a, ALU.mult)
                step(v.tensor_reduce(node[:, :, 1], tmp, AX, ALU.add))
                ts(node[:, :, 1], node[:, :, 1], 1.0 / D, EPS, ALU.mult, ALU.add)
                ask_root()
                step(v.reciprocal(node[:, :, 1], node[:, :, 1]))
                tt(o, a, deg(node[:, :, 1]), ALU.mult)

            step(v.memset(pad[:, 0, :], 0))
            step(v.memset(pad[:, 1, :], NO_NODE))
            step(v.memset(X[:, T - 1, :], 0.0))
            step(v.memset(part[:], 0.0))
            step(v.memset(B4[:], 0.0))
            reach("pad")
            dve.wait_ge(s_bcast, 1)
            step(v.tensor_copy(vec[:].rearrange("p n f -> p (n f)"), bank(0, 2)[:, 0:len(VECS) * D]))
            reach("vec")
            dve.wait_ge(s_in, N_IN)
            step(v.tensor_scalar(last_i[:], last_i[:], 7, None, ALU.arith_shift_right))
            step(v.tensor_copy(last_f[:], last_i[:]))
            tt(last_f[:], last_f[:], cnum[:], ALU.add)
            reach("vsteps")
            dve.wait_ge(s_vrow, 1)
            for b in range(KB):
                step(v.tensor_scalar(ck_junk[:], bank(2, 4)[:, 0:C - 1], kcol[:, b:b + 1], 0.0, ALU.is_le, ALU.add,
                                     accum_out=ck[:, b:b + 1]))
            step(v.tensor_copy(ck_i[:], ck[:]))
            reach("ck")
            tt(dk[:], kcol[:], ck[:], ALU.subtract)
            ts(ck[:], dk[:], float(T - 1), None, ALU.min)
            step(v.tensor_copy(dk_i[:], ck[:]))
            reach("dk")
            ts(dk[:], dk[:], float(P), None, ALU.mult)
            dve.wait_ge(s_chunks, 16 * KB)
            step(v.tensor_copy(G_f[:], G_i[:]))
            tt(G_f[:, :, P:2 * P], G_f[:, :, P:2 * P], dk[:].unsqueeze(2).to_broadcast([P, KB, P]), ALU.subtract)
            reach("chunks")
            dve.wait_ge(s_tr, 1)
            step(v.tensor_copy(src_i[:], bank(0, 4)[:, 0:K]))
            ts(srcm[:], bank(0, 4)[:, 0:K], trash[:, 0:1], None, ALU.subtract)
            step(v.tensor_copy(dloc[:], bank(4, 4)[:, 0:K]))
            ts(mask[:], dloc[:], 0.0, None, ALU.is_ge)
            step(v.scalar_tensor_tensor(mask[:], dloc[:], P - 0.5, mask[:], ALU.is_le, ALU.mult))
            tt(srcm[:], srcm[:], mask[:], ALU.mult)
            ts(srcm[:], srcm[:], trash[:, 0:1], None, ALU.add)
            dve.wait_ge(s_dma, 32)
            low_i = G_i.rearrange("p b e -> p (b e)")[:, 0:K]
            low_f = G_f.rearrange("p b e -> p (b e)")[:, 0:K]
            step(v.tensor_copy(low_i, srcm[:]))
            step(v.tensor_scalar(low_i, low_i, P - 1, None, ALU.bitwise_and))
            step(v.tensor_copy(low_f, low_i))
            step(v.tensor_copy(src_split[:, 1, :], low_f))
            tt(src_split[:, 0, :], srcm[:], low_f, ALU.subtract)
            step(v.tensor_copy(ident_b[:], ident[:]))
            step(v.memset(acc[:], 0.0))
            reach("agg1")
            dve_segsum(dve, "agg1", D + 1)
            ts(wdeg[:], acc[:, :, D], 1.0, None, ALU.add)
            tt(B1[:], X[:], acc[:, :, 0:D], ALU.add)
            reach("h_in")
            dve_linear(dve, "h", [(B2, 0, "L0_b1")])
            reach("hid")
            step(v.memset(acc[:], 0.0))
            reach("agg2")
            dve_segsum(dve, "agg2", D)
            tt(B1[:], B2[:], acc[:, :, 0:D], ALU.add)
            reach("out0_in")
            dve_linear(dve, "out0", [(B3, 0, "L0_b2")])
            tt(B3[:], B3[:], X[:], ALU.add)
            layer_norm(X1[:], B3[:], B1[:])
            reach("x1")
            dve_linear(dve, "pv", [(B1, 0, None), (B2, D, None)])
            center(B1[:], N)
            step(v.tensor_copy(acc[:, :, 0:D], B1[:]))
            step(v.tensor_copy(acc[:, :, D:2 * D], B2[:]))
            tt(acc[:, :, 2 * D:], B1[:], B1[:], ALU.mult)
            reach("pv_rows")
            dve.wait_ge(s_dma, 80)
            step(v.memset(acc[:], 0.0))
            reach("pv")
            dve_segsum(dve, "pv", 3 * D)
            tt(B2[:], B2[:], acc[:, :, D:2 * D], ALU.add)
            tt(B2[:], B2[:], wide(vec[:, VECS.index("b_unite"), :]), ALU.add)
            center(B2[:], N)
            tt(B3[:], B1[:], acc[:, :, 0:D], ALU.add)
            fold(0, B3[:])
            tt(B3[:], B3[:], B2[:], ALU.mult)
            fold(4, B3[:])
            tt(B3[:], B1[:], B1[:], ALU.mult)
            tt(B3[:], B3[:], acc[:, :, 2 * D:], ALU.add)
            fold(1, B3[:])
            tt(B3[:], B2[:], deg(wdeg[:]), ALU.mult)
            fold(2, B3[:])
            tt(B3[:], B3[:], B2[:], ALU.mult)
            fold(3, B3[:])
            ask_sums()
            step(v.tensor_copy(nrm[:, 8, :], total(2)))
            tt(nrm[:, 8, :], nrm[:, 8, :], total(0), ALU.add)
            ts(nrm[:, 8, :], nrm[:, 8, :], 1.0 / ROWS, None, ALU.mult)
            step(v.tensor_copy(nrm[:, 0, :], total(4)))
            ts(nrm[:, 0, :], nrm[:, 0, :], 2.0, None, ALU.mult)
            tt(nrm[:, 0, :], nrm[:, 0, :], total(1), ALU.add)
            tt(nrm[:, 0, :], nrm[:, 0, :], total(3), ALU.add)
            ts(nrm[:, 0, :], nrm[:, 0, :], 1.0 / ROWS, None, ALU.mult)
            tt(nrm[:, 9, :], nrm[:, 8, :], nrm[:, 8, :], ALU.mult)
            tt(nrm[:, 0, :], nrm[:, 0, :], nrm[:, 9, :], ALU.subtract)
            scale_of(nrm[:, 0, :], "g1", nrm[:, 0, :])
            tt(nrm[:, 9, :], nrm[:, 8, :], nrm[:, 0, :], ALU.mult)
            tt(nrm[:, 1, :], vec[:, VECS.index("be1"), :], nrm[:, 9, :], ALU.subtract)
            tt(B3[:], B2[:], wide(nrm[:, 0, :]), ALU.mult)
            tt(B3[:], B3[:], wide(nrm[:, 1, :]), ALU.add)
            tt(B4[:], B1[:], wide(nrm[:, 0, :]), ALU.mult)
            tt(B4[:], B4[:], B3[:], ALU.add)
            ts(B4[:], B4[:], 0.0, None, ALU.max)
            clear_tail(B4[:])
            step(v.memset(acc[:], 0.0))
            reach("edges1")
            with dve.Fori(0, ITER) as i:
                tiles = load_tiles(ENG.DVE, i)
                for h in range(2):
                    reuse(dve, e1_seg, i, h)
                    one_hots(i, h).then_inc(e1_oh[h], 1)
                for h in range(2):
                    dve.wait_ge(e1_saved[h], i * 16 + 16)
                    dve.wait_ge(e1_in[h], i * 16 * G + 16 * G)
                    v.tensor_tensor(hm[:, h], work[:, h], nrm[:, 0, :].unsqueeze(1).to_broadcast([P, G, D]),
                                    ALU.mult).then_inc(e1_used[h], 1)
                    done(dve, e1_used, i, h)
                    done(dve, e1_q, i, h)
                    v.tensor_tensor(hm[:, h], hm[:, h], bank(4 + h).rearrange("p (g f) -> p g f", f=D),
                                    ALU.add).then_inc(e1_chain, 1)
                    dve.wait_ge(e1_chain, i * 2 + h + 1)
                    v.scalar_tensor_tensor(hm[:, h], hm[:, h], 0.0,
                                           mask[:, bass.ds(i * 2 * G + h * G, G)].unsqueeze(2).to_broadcast([P, G, D]),
                                           ALU.max, ALU.mult).then_inc(e1_hm[h], 1)
                for h in range(2):
                    done(dve, e1_seg, i, h)
                    add_steps(dve, i, h, tiles, e1_added, lambda j: bank(4 + h)[:, D * j:D * j + D], D)
            dve.wait_ge(e1_added, ITER * 2 * G + 1)
            tt(B1[:], acc[:, :, 0:D], B4[:], ALU.add)
            step(v.tensor_copy(gram[:], bank(6)[0:D, 0:D]))
            dve.sem_inc(s_gram, 1)
            reach("s")
            dve_linear(dve, "SW", [(B3, 0, None)])
            reach("HW_in")
            dve_linear(dve, "HW", [(X, 0, None)])
            step(v.memset(acc[:], 0.0))
            reach("msg")
            dve_segsum(dve, "msg", D)
            dve.wait_ge(s_dma, 96)
            step(v.tensor_copy(B1[:], acc[:, :, 0:D]))
            reach("U_in")
            dve_linear(dve, "U", [(B4, 0, "b_gconv")])
            center(B4[:], N)
            fold(0, B3[:])
            tt(B3[:], B3[:], B4[:], ALU.mult)
            fold(3, B3[:])
            tt(B3[:], B4[:], deg(wdeg[:]), ALU.mult)
            fold(1, B3[:])
            tt(B3[:], B3[:], B4[:], ALU.mult)
            fold(2, B3[:])
            reach("gram")
            dve.wait_ge(s_gw, 1)
            step(v.memset(part[:, 4, :], 0.0))
            tt(part[0:D, 4, :], bank(5)[0:D, 0:D], M("WgH"), ALU.mult)
            ask_sums()
            step(v.tensor_copy(nrm[:, 8, :], total(0)))
            tt(nrm[:, 8, :], nrm[:, 8, :], total(1), ALU.add)
            ts(nrm[:, 8, :], nrm[:, 8, :], 1.0 / ROWS, None, ALU.mult)
            step(v.tensor_copy(nrm[:, 2, :], total(3)))
            ts(nrm[:, 2, :], nrm[:, 2, :], 2.0, None, ALU.mult)
            tt(nrm[:, 2, :], nrm[:, 2, :], total(2), ALU.add)
            tt(nrm[:, 2, :], nrm[:, 2, :], total(4), ALU.add)
            ts(nrm[:, 2, :], nrm[:, 2, :], 1.0 / ROWS, None, ALU.mult)
            tt(nrm[:, 9, :], nrm[:, 8, :], nrm[:, 8, :], ALU.mult)
            tt(nrm[:, 2, :], nrm[:, 2, :], nrm[:, 9, :], ALU.subtract)
            scale_of(nrm[:, 2, :], "g2", nrm[:, 2, :])
            tt(nrm[:, 9, :], nrm[:, 8, :], nrm[:, 2, :], ALU.mult)
            tt(nrm[:, 3, :], vec[:, VECS.index("be2"), :], nrm[:, 9, :], ALU.subtract)
            tt(w2[:], M("WgH"), nrm[0:D, 2, :], ALU.mult)
            tt(B4[:], B4[:], wide(nrm[:, 2, :]), ALU.mult)
            tt(B4[:], B4[:], wide(nrm[:, 3, :]), ALU.add)
            tt(X[:], X[:], wide(nrm[:, 2, :]), ALU.mult)
            tt(X[:], X[:], B4[:], ALU.add)
            ts(X[:], X[:], 0.0, None, ALU.max)
            reach("edges2")
            with dve.Fori(0, ITER) as i:
                for h in range(2):
                    ks = bass.ds(i * 2 * G + h * G, G)
                    reuse(dve, e2_row, i, h)
                    v.tensor_copy(src_b[:, h], src_split[:, :, ks]).then_inc(e2_src[h], 1)
                    reuse(dve, e2_T, i, h)
                    one_hots(i, h, oh_b).then_inc(e2_oh[h], 1)
                    done(dve, e2_row, i, h)
                    reuse(dve, e2_sum, i, h)
                    v.tensor_tensor(eq[:, h], bank(5, 2).rearrange("p (g e) -> p g e", e=P),
                                    srcm[:, ks].unsqueeze(2).to_broadcast([P, G, P]), ALU.is_equal
                                    ).then_inc(e2_eq[h], 1)
                    done(dve, e2_eq, i, h)
                    v.tensor_tensor(before[:], eq[:, h], tri[:].unsqueeze(1).to_broadcast([P, G, P]), ALU.mult
                                    ).then_inc(e2_chain, 1)
                    dve.wait_ge(e2_chain, i * 8 + 4 * h + 1)
                    v.tensor_reduce(dup[:, h], before[:], AX, ALU.add).then_inc(e2_chain, 1)
                    dve.wait_ge(e2_chain, i * 8 + 4 * h + 2)
                    v.tensor_scalar(dup[:, h], dup[:, h], 0.0, None, ALU.is_equal).then_inc(e2_chain, 1)
                    reuse(dve, e2_idx, i, h)
                    dve.wait_ge(e2_chain, i * 8 + 4 * h + 3)
                    v.scalar_tensor_tensor(idx_f[:, h], srcm[:, ks], trash[:, 0:1], dup[:, h], ALU.subtract, ALU.mult
                                           ).then_inc(e2_chain, 1)
                    dve.wait_ge(e2_chain, i * 8 + 4 * h + 4)
                    v.tensor_scalar(idx_f[:, h], idx_f[:, h], trash[:, 0:1], None, ALU.add).then_inc(e2_ixf[h], 1)
            for h in range(2):
                dve.wait_ge(e2_sum[h], ITER + 1)
            step(v.tensor_copy(acc[:, :, 0:D], X[:]))
            step(v.tensor_copy(acc[:, :, D:2 * D], X[:]))
            for j in range(G):
                dve.wait_ge(tab_in[j % 2], 16 * (j // 2 + 1))
                tt(acc[:, :, D:2 * D], acc[:, :, D:2 * D], [B1, B3][j % 2][:], ALU.add)
                reach(f"table{j}")
            reach("t_in")
            dve_linear(dve, "t", [(B1, 0, "b_transfer")])
            node_norm(B1[:], "g2", "be2", B3[:])
            reach("lin_in")
            dve_linear(dve, "lin", [(B2, 0, "b_lin")])
            ts(B2[:], B2[:], 0.0, None, ALU.max)
            node_norm(B2[:], "g3", "be3", B3[:])
            tt(B2[:], B2[:], X1[:], ALU.add)
            layer_norm(B1[:], B2[:], B3[:])
            reach("out")


_INS = ["x", "src", "dst"]
_PRE = {"L0_b1": "L0_gnn_b1", "L0_b2": "L0_gnn_b2"}


def kernel(**inputs):
    import numpy as _np
    import concourse.bacc as _bacc
    from concourse import mybir as _mybir
    from concourse.bass_utils import run_bass_kernel_spmd as _run

    a = {k: _np.ascontiguousarray(v) for k, v in inputs.items()}
    unite, gconv = a["L1_gnn_W_unite"], a["L1_gnn_W_gconv"]
    mats = _np.stack([a["L0_gnn_W1"], a["L0_gnn_W2"], unite[:D], unite[D:], gconv[:D], gconv[D:], a["L1_gnn_W_lin"]])
    vecs = _np.concatenate([a[_PRE.get(n, "L1_gnn_" + n)] for n in VECS])[None, :]
    arrays = {"in_x": a["x"], "in_src": a["src"], "in_dst": a["dst"], "in_mats": mats, "in_vecs": vecs,
              "in_w_transfer": a["L1_gnn_W_transfer"]}
    nc = _bacc.Bacc("TRN2", target_bir_lowering=False, num_devices=1)
    args = [nc.dram_tensor(n, v.shape, _mybir.dt.from_np(v.dtype), kind="ExternalInput").ap() for n, v in arrays.items()]
    out = nc.dram_tensor("out", (N, D), F32, kind="ExternalOutput").ap()
    build(nc, *args, out)
    r = _run(nc, [arrays], core_ids=[0])
    return r.results[0]["out"]
```
